# Optimizing a Trainium2 kernel written in Bass

```python
import numpy as np
import jax
import jax.numpy as jnp

def _softmax(x, axis=-1):
    return jax.nn.softmax(x, axis=axis)

def _gelu(x):
    return jax.nn.gelu(x, approximate=True)

def _silu(x):
    return jax.nn.silu(x)

def _sigmoid(x):
    return jax.nn.sigmoid(x)

def _layernorm(x, axis=-1, eps=1e-05):
    m = jnp.mean(x, axis=axis, keepdims=True)
    v = jnp.var(x, axis=axis, keepdims=True)
    return (x - m) / jnp.sqrt(v + eps)

def _scatter_add(tgt, idx, src, axis=0):
    return tgt.at[idx].add(src)

def _segment_sum(src, seg, n):
    return jax.ops.segment_sum(src, seg, n)
kernel_name = 'mk_decoder_postln_d1_seqx_r4_bba02d'

def setup_inputs(seed: int=0):
    np.random.seed(seed)
    _w = jnp.asarray

    def _rec_inputs():
        import jax
        import jax.numpy as jnp
        _rk = jax.random.key(seed)
        x = 0.0003765 + 1 * jax.random.normal(jax.random.fold_in(_rk, 1), (8, 256, 512), jnp.float32)
        _lenS = 256 - jax.random.randint(jax.random.fold_in(_rk, 7), (8,), 0, max(1, 256 // 4) + 1, jnp.int32)
        _lenS2 = 256 - jax.random.randint(jax.random.fold_in(_rk, 8), (8,), 0, max(1, 256 // 4) + 1, jnp.int32)
        _ctx_2048P = jax.random.normal(jax.random.fold_in(_rk, 11), (8, 16, 512), jnp.float32)
        _ctx_2048c = jax.random.dirichlet(jax.random.fold_in(_rk, 511), 0.3 * jnp.ones((16,), jnp.float32), (8, 256))
        _ctx_2048t = jnp.einsum('bsk,bkd->bsd', _ctx_2048c, _ctx_2048P)
        _ctx_2048t = _ctx_2048t * jax.lax.rsqrt(jnp.mean(jnp.square(_ctx_2048t)) + 1e-12) * 0.953939
        ctx_2048 = -0.000292821 + 1.00034 * (_ctx_2048t + 0.3 * jax.random.normal(jax.random.fold_in(_rk, 611), (8, 256, 512), jnp.float32))
        return (x, ctx_2048)
    x, ctx_2048 = _rec_inputs()

    def _L0_attn_setup():
        import jax, jax.numpy as jnp
        import numpy as np
        EPS = 1e-06

        def _sigma(x):
            return jax.nn.elu(x) + 1.0

        def _reference_tuple_inner(hidden_states, w_q, w_k, w_v, w_o, gate, M, z):
            q = jnp.einsum('bsh,dh->bsd', hidden_states, w_q)
            k = jnp.einsum('bsh,dh->bsd', hidden_states, w_k)
            v = jnp.einsum('bsh,dh->bsd', hidden_states, w_v)
            sq = _sigma(q)
            mem_num = jnp.einsum('bsd,de->bse', sq, M)
            mem_den = jnp.einsum('bsd,d->bs', sq, z) + EPS
            memory_output = mem_num / mem_den[..., None]
            pq, pk = (_sigma(q), _sigma(k))
            kv_cum = jnp.cumsum(jnp.einsum('bsd,bse->bsde', pk, v), axis=1)
            k_cum = jnp.cumsum(pk, axis=1)
            num = jnp.einsum('bsd,bsde->bse', pq, kv_cum)
            den = jnp.einsum('bsd,bsd->bs', pq, k_cum) + EPS
            local_output = num / den[..., None]
            g = jax.nn.sigmoid(gate)
            output = g * memory_output + (1.0 - g) * local_output
            sk = _sigma(k)
            v_ret = jnp.einsum('bsd,de->bse', sk, M) / (jnp.einsum('bsd,d->bs', sk, z) + EPS)[..., None]
            M_new = M + jnp.einsum('bsd,bse->de', sk, v - v_ret)
            z_new = z + jnp.sum(sk, axis=(0, 1))
            out = jnp.einsum('bsd,hd->bsh', output, w_o)
            return (out, M_new, z_new)
        key = jax.random.key(seed)
        ks = jax.random.split(key, 8)
        B, S, H, D = (2, 1024, 512, 128)
        sc = 1.0 / np.sqrt(H)
        return {'hidden_states': jax.random.normal(ks[0], (B, S, H), jnp.float32), 'w_q': jax.random.normal(ks[1], (D, H), jnp.float32) * sc, 'w_k': jax.random.normal(ks[2], (D, H), jnp.float32) * sc, 'w_v': jax.random.normal(ks[3], (D, H), jnp.float32) * sc, 'w_o': jax.random.normal(ks[4], (H, D), jnp.float32) * (1.0 / np.sqrt(D)), 'gate': jnp.zeros((1,), jnp.float32), 'M': jax.random.normal(ks[5], (D, D), jnp.float32), 'z': jax.random.uniform(ks[6], (D,), jnp.float32) + 0.5}
    _L0_attn_all = _L0_attn_setup()
    _L0_attn_in = {k: v for k, v in _L0_attn_all.items() if k in ('w_q', 'w_k', 'w_v', 'w_o', 'gate', 'M', 'z')}
    del _L0_attn_all

    def _L0_xattn_setup():
        import jax, jax.numpy as jnp
        import numpy as np
        key = jax.random.key(seed)
        k1, k2, k3, k4, k5 = jax.random.split(key, 5)
        B, D_MODEL, L = (2, 256, 512)
        HEAD_DIM = 8
        H = D_MODEL // HEAD_DIM
        return {'k': jax.random.normal(k1, (B, D_MODEL, L), dtype=jnp.float32), 'v': jax.random.normal(k2, (B, D_MODEL, L), dtype=jnp.float32), 'q': jax.random.normal(k3, (B, D_MODEL, L), dtype=jnp.float32), 'ssm_kernel': jax.random.normal(k4, (H, L), dtype=jnp.float32), 'D': jax.random.normal(k5, (H,), dtype=jnp.float32), 'head_dim': HEAD_DIM}
    _L0_xattn_all = _L0_xattn_setup()
    _L0_xattn_in = {k: v for k, v in _L0_xattn_all.items() if k in ('ssm_kernel', 'D')}
    del _L0_xattn_all

    def _L0_ffn_setup():
        import jax, jax.numpy as jnp
        import numpy as np
        _FP4_LUT = jnp.array([0.0, 0.5, 1.0, 1.5, 2.0, 3.0, 4.0, 6.0, -0.0, -0.5, -1.0, -1.5, -2.0, -3.0, -4.0, -6.0], dtype=jnp.float32)
        GROUP_SIZE = 128
        EPS = 1e-06

        def _dequant_fp4(packed_i32, scales_f16, group_size):
            out_f, in_p = packed_i32.shape
            w = packed_i32.astype(jnp.uint32)
            shifts = jnp.arange(8, dtype=jnp.uint32) * 4
            nib = w[:, :, None] >> shifts & jnp.uint32(15)
            vals = _FP4_LUT[nib.astype(jnp.int32)].reshape(out_f, in_p * 8)
            s = scales_f16.astype(jnp.float32).T
            s_full = jnp.repeat(s, group_size, axis=1)
            return vals * s_full
        key = jax.random.key(seed)
        k1, k2, k3, k4, k5 = jax.random.split(key, 5)
        B, S, H, I = (4, 512, 512, 1408)
        x = jax.random.normal(k1, (B, S, H), dtype=jnp.float32)
        gate_up_packed = jax.random.randint(k2, (2 * I, H // 8), 0, 2147483647, dtype=jnp.int32)
        gate_up_scales = jax.random.uniform(k3, (H // GROUP_SIZE, 2 * I), dtype=jnp.float32).astype(jnp.float16)
        down_packed = jax.random.randint(k4, (H, I // 8), 0, 2147483647, dtype=jnp.int32)
        down_scales = jax.random.uniform(k5, (I // GROUP_SIZE, H), dtype=jnp.float32).astype(jnp.float16)
        return {'x': x, 'gate_up_packed': gate_up_packed, 'gate_up_scales': gate_up_scales, 'down_packed': down_packed, 'down_scales': down_scales}
    _L0_ffn_all = _L0_ffn_setup()
    _L0_ffn_in = {k: v for k, v in _L0_ffn_all.items() if k in ('gate_up_packed', 'gate_up_scales', 'down_packed', 'down_scales')}
    del _L0_ffn_all
    return {'x': x, 'ctx_2048': ctx_2048, 'L0_attn_w_q': _L0_attn_in['w_q'], 'L0_attn_w_k': _L0_attn_in['w_k'], 'L0_attn_w_v': _L0_attn_in['w_v'], 'L0_attn_w_o': _L0_attn_in['w_o'], 'L0_attn_gate': _L0_attn_in['gate'], 'L0_attn_M': _L0_attn_in['M'], 'L0_attn_z': _L0_attn_in['z'], 'L0_xattn_ssm_kernel': _L0_xattn_in['ssm_kernel'], 'L0_xattn_D': _L0_xattn_in['D'], 'L0_ffn_gate_up_packed': _L0_ffn_in['gate_up_packed'], 'L0_ffn_gate_up_scales': _L0_ffn_in['gate_up_scales'], 'L0_ffn_down_packed': _L0_ffn_in['down_packed'], 'L0_ffn_down_scales': _L0_ffn_in['down_scales']}

def reference(x, ctx_2048, L0_attn_w_q, L0_attn_w_k, L0_attn_w_v, L0_attn_w_o, L0_attn_gate, L0_attn_M, L0_attn_z, L0_xattn_ssm_kernel, L0_xattn_D, L0_ffn_gate_up_packed, L0_ffn_gate_up_scales, L0_ffn_down_packed, L0_ffn_down_scales):
    import jax
    import jax.numpy as jnp

    def _L0_attn_ref(hidden_states, w_q, w_k, w_v, w_o, gate, M, z):
        import jax, jax.numpy as jnp
        import numpy as np
        EPS = 1e-06

        def _sigma(x):
            return jax.nn.elu(x) + 1.0

        def _reference_tuple_inner(hidden_states, w_q, w_k, w_v, w_o, gate, M, z):
            q = jnp.einsum('bsh,dh->bsd', hidden_states, w_q)
            k = jnp.einsum('bsh,dh->bsd', hidden_states, w_k)
            v = jnp.einsum('bsh,dh->bsd', hidden_states, w_v)
            sq = _sigma(q)
            mem_num = jnp.einsum('bsd,de->bse', sq, M)
            mem_den = jnp.einsum('bsd,d->bs', sq, z) + EPS
            memory_output = mem_num / mem_den[..., None]
            pq, pk = (_sigma(q), _sigma(k))
            kv_cum = jnp.cumsum(jnp.einsum('bsd,bse->bsde', pk, v), axis=1)
            k_cum = jnp.cumsum(pk, axis=1)
            num = jnp.einsum('bsd,bsde->bse', pq, kv_cum)
            den = jnp.einsum('bsd,bsd->bs', pq, k_cum) + EPS
            local_output = num / den[..., None]
            g = jax.nn.sigmoid(gate)
            output = g * memory_output + (1.0 - g) * local_output
            sk = _sigma(k)
            v_ret = jnp.einsum('bsd,de->bse', sk, M) / (jnp.einsum('bsd,d->bs', sk, z) + EPS)[..., None]
            M_new = M + jnp.einsum('bsd,bse->de', sk, v - v_ret)
            z_new = z + jnp.sum(sk, axis=(0, 1))
            out = jnp.einsum('bsd,hd->bsh', output, w_o)
            return (out, M_new, z_new)
        return _reference_tuple_inner(hidden_states, w_q, w_k, w_v, w_o, gate, M, z)[0]

    def _L0_xattn_ref(k, v, q, ssm_kernel, D, head_dim):
        import jax, jax.numpy as jnp
        import numpy as np
        B, HD, L = k.shape
        H = HD // head_dim
        fft_size = 2 * L
        k_ = k.reshape(B, H, head_dim, L)
        v_ = v.reshape(B, H, head_dim, L)
        q_ = q.reshape(B, H, head_dim, L)
        kv = jnp.einsum('bhil,bhjl->bijhl', k_, v_)
        kv_f = jnp.fft.rfft(kv, n=fft_size)
        kernel_f = jnp.fft.rfft(ssm_kernel, n=fft_size)
        y = jnp.fft.irfft(kv_f * kernel_f, n=fft_size)[..., :L]
        out = y + kv * D[None, None, None, :, None]
        out = jnp.einsum('bijhl,bhil->bjhl', out, q_)
        out = jnp.transpose(out, (0, 2, 1, 3)).reshape(B, H * head_dim, L)
        return out.astype(k.dtype)

    def _L0_ffn_ref(x, gate_up_packed, gate_up_scales, down_packed, down_scales):
        import jax, jax.numpy as jnp
        import numpy as np
        _FP4_LUT = jnp.array([0.0, 0.5, 1.0, 1.5, 2.0, 3.0, 4.0, 6.0, -0.0, -0.5, -1.0, -1.5, -2.0, -3.0, -4.0, -6.0], dtype=jnp.float32)
        GROUP_SIZE = 128
        EPS = 1e-06

        def _dequant_fp4(packed_i32, scales_f16, group_size):
            out_f, in_p = packed_i32.shape
            w = packed_i32.astype(jnp.uint32)
            shifts = jnp.arange(8, dtype=jnp.uint32) * 4
            nib = w[:, :, None] >> shifts & jnp.uint32(15)
            vals = _FP4_LUT[nib.astype(jnp.int32)].reshape(out_f, in_p * 8)
            s = scales_f16.astype(jnp.float32).T
            s_full = jnp.repeat(s, group_size, axis=1)
            return vals * s_full
        I = gate_up_packed.shape[0] // 2
        w_gu = _dequant_fp4(gate_up_packed, gate_up_scales, GROUP_SIZE)
        w_down = _dequant_fp4(down_packed, down_scales, GROUP_SIZE)
        gate_up = jnp.einsum('bsh,oh->bso', x, w_gu)
        gate, up = (gate_up[..., :I], gate_up[..., I:])
        h = jax.nn.silu(gate) * up
        y = jnp.einsum('bsi,hi->bsh', h, w_down)
        rms = jnp.sqrt(jnp.mean(y * y, axis=-1, keepdims=True) + EPS)
        return y / rms
    x = _layernorm(x + _L0_attn_ref(x, L0_attn_w_q, L0_attn_w_k, L0_attn_w_v, L0_attn_w_o, L0_attn_gate, L0_attn_M, L0_attn_z), axis=-1)
    x = _layernorm(x + _L0_xattn_ref(ctx_2048, ctx_2048, x, L0_xattn_ssm_kernel, L0_xattn_D, 8), axis=-1)
    x = _layernorm(x + _L0_ffn_ref(x, L0_ffn_gate_up_packed, L0_ffn_gate_up_scales, L0_ffn_down_packed, L0_ffn_down_scales), axis=-1)
    return x

_drawn_inputs = setup_inputs


def setup_inputs(seed=0):
    import zlib

    import numpy as np

    out = dict(_drawn_inputs(seed))
    spreads = {}
    factors = {}
    for name, (base, spread) in spreads.items():
        noise = np.random.default_rng([zlib.crc32(name.encode()), seed]).standard_normal(out[name].shape)
        drawn = base * np.exp(spread * noise) if base else spread * noise
        out[name] = jnp.asarray(drawn.astype(out[name].dtype))
    for name, factor in factors.items():
        out[name] = (out[name] * factor).astype(out[name].dtype)
    return out
```

```python
from contextlib import ExitStack

import concourse.bass as bass
from concourse import mybir

ALU = mybir.AluOpType
ACT = mybir.ActivationFunctionType
F32 = mybir.dt.float32
F16 = mybir.dt.float16
U32 = mybir.dt.uint32

P = 128
LN_EPS = 1e-5
DEN_EPS = 1e-6
RMS_EPS = 1e-6
H_SHIFT = 2.0 ** -8
FP4_SHIFT = 2.0 ** 14


def at(index, per, k):
    return index * per + k


def wait(engine, semaphore, value):
    if isinstance(value, int) and value <= 0:
        return
    engine.wait_ge(semaphore, value)


def rounds(engine, body, first, last, looped_from, looped_to):
    for i in range(first, looped_from):
        body(i)
    with engine.Fori(looped_from, looped_to + 1) as i:
        body(i)
    for i in range(looped_to + 1, last + 1):
        body(i)


def attention_and_weights(nc, sb, keep, x, wq, wk, wv, wo, gate, M, z, ssm, ssm_d, gu_packed, gu_scales, dn_packed,
                          dn_scales, toeplitz_rows, stack):
    B, S, D = x.shape
    DH = wq.shape[0]
    KD = D // P
    TT = S // P
    OG = gu_packed.shape[0] // P
    GI = dn_scales.shape[0]
    NH = ssm.shape[0]
    LP = toeplitz_rows.shape[-1]
    WG = D // 8
    WD = P // 8
    assert (KD, TT, OG, GI, B) == (4, 2, 22, 11, 8)

    def sem(name):
        return stack.enter_context(nc.semaphore(name))

    def psum(name):
        return stack.enter_context(nc.psum_tensor(name, [P, 512], F32))

    ident = keep["ident"]
    x1T = keep["x1T"]

    rows4 = sb("rows4", [P, 4, D], F32)
    wnat = rows4[:, 0:3, :]
    wonat = rows4[:, 3, :].rearrange("p (t d) -> p t d", t=KD)
    zs, x1n = rows4[:, 0:TT, :], rows4[:, TT:2 * TT, :]
    wT = sb("wT", [P, 3, KD, DH], F32)
    woT = sb("woT", [P, D], F32)
    Mz = sb("Mz", [P, DH + 1], F32)
    gates = sb("gates", [P, 4], F32)
    gtmp = sb("gtmp", [P, 4], F32)
    mask = sb("mask", [P, 3 * P], F32)
    halfneg = keep["halfneg"]
    srow_g = sb("srow_g", [KD * OG, P], F16)
    srow_d = sb("srow_d", [GI * 4, P], F16)
    srow_gf = sb("srow_gf", [KD * OG, P], F32)
    srow_df = sb("srow_df", [GI * 4, P], F32)
    sc_g = sb("sc_g", [P, KD, OG], F32)
    sc_d = sb("sc_d", [P, GI, 4], F32)
    pk_g = sb("pk_g", [P, OG * WG], U32)
    pk_d = sb("pk_d", [P, 4 * GI * WD], U32)
    sgn = sb("sgn", [P, OG * WG], U32)
    pk_dg = sgn[:, OG * WG // 2:OG * WG]
    mag = sb("mag", [P, OG * WG], U32)
    v_g = sb("v_g", [P, OG * D], F16)
    v_d = sb("v_d", [P, GI * 512], F16)
    w32 = sb("w32", [P, 2, 512], F32)
    kin = sb("kin", [NH, 512], F32)
    kd = sb("kd", [NH, 1], F32)
    kpad = sb("kpad", [NH, 2, LP], F16)
    xin = sb("xin", [P, TT, D], F32)
    xres = sb("xres", [P, TT, D], F32)
    xT = sb("xT", [P, KD, S], F32)
    neg = sb("neg", [P, 2 * S], F32)
    sqk = sb("sqk", [P, 2 * S], F32)
    vext = sb("vext", [P, TT, DH + 1], F32)
    AT = sb("AT", [P, 3 * P], F32)
    den = sb("den", [P, 4], F32)
    rden = sb("rden", [P, 4], F32)
    coef = sb("coef", [P, 4], F32)
    loc = sb("loc", [P, TT, DH], F32)
    o = sb("o", [P, TT, DH], F32)
    oT = sb("oT", [P, S], F32)
    st = sb("st", [P, TT, 6], F32)
    mv = sb("mv", [P, TT, 2], F32)
    ve = sb("ve", [P, TT], F32)
    rs = sb("rs", [P, TT], F32)

    tr = [psum("p_tr0"), psum("p_tr1")]
    p_qk, p_v, p_sc, p_out = psum("p_qk"), psum("p_v"), psum("p_sc"), psum("p_out")
    p_nm = [psum("p_nm0"), psum("p_nm1")]

    in_w, in_wo, in_mz, in_gate = sem("in_w"), sem("in_wo"), sem("in_mz"), sem("in_gate")
    in_sc, in_pg, in_pd, in_k = sem("in_sc"), sem("in_pg"), sem("in_pd"), sem("in_k")
    in_x, in_res = sem("in_x"), sem("in_res")
    masks_made = sem("masks_made")
    wts_transposed, wts_kept = sem("wts_transposed"), sem("wts_kept")
    consts = sem("consts")
    kernel_split = sem("kernel_split")
    rows_stored = sem("rows_stored")
    unpacked = sem("unpacked")
    gate_exp = sem("gate_exp")
    x_transposed, xT_a, xT_v = sem("x_transposed"), sem("xT_a"), sem("xT_v")
    qk_done, v_done = sem("qk_done"), sem("v_done")
    neg_made, exp_made, sqk_made, v_kept = sem("neg_made"), sem("exp_made"), sem("sqk_made"), sem("v_kept")
    scores_done, masked = sem("scores_done"), sem("masked")
    sums_done, o_steps = sem("sums_done"), sem("o_steps")
    o_transposed, oT_kept = sem("o_transposed"), sem("oT_kept")
    proj_done, z_made = sem("proj_done"), sem("z_made")
    seen = sem("seen")
    stats, rs_made, x1_made = sem("stats"), sem("rs_made"), sem("x1_made")
    x1_transposed, x1T_kept = sem("x1_transposed"), sem("x1T_kept")
    w_scaled, w_transposed, w_high, w_low = sem("w_scaled"), sem("w_transposed"), sem("w_high"), sem("w_low")

    LOOP = (2, 6)

    def has(i, lo, hi):
        return not isinstance(i, int) or lo <= i <= hi

    def weight_tiles(i):
        if isinstance(i, int):
            table = {1: (0, "gg"), 7: (22, "gggd"), 8: (26, "ggdd"), 9: (30, "ddd")}
            if i not in table and not LOOP[0] <= i <= LOOP[1]:
                return []
        else:
            table = {}
        n0, kinds = table.get(i, (i * 4 - 6, "gggd")) if isinstance(i, int) else (i * 4 - 6, "gggd")
        g0 = 0 if isinstance(i, int) and i == 1 else i * 3 - 4
        d0 = {8: 6, 9: 8}.get(i, i - 2) if isinstance(i, int) else i - 2
        out, g, d = [], 0, 0
        for k, kind in enumerate(kinds):
            if kind == "g":
                out.append((n0 + k, k, "g", g0 + g))
                g += 1
            else:
                out.append((n0 + k, k, "d", d0 + d))
                d += 1
        return out

    with nc.Block() as block:

        @block.sync
        def _(sp):
            sp.dma_start(xin[:], x[0].rearrange("(t p) d -> p t d", p=P)).then_inc(in_x, 16)
            for m, w in enumerate((wq, wk, wv)):
                sp.dma_start(wnat[:, m, :], w).then_inc(in_w, 16)
            sp.dma_start(wonat, wo.rearrange("(t p) d -> p t d", p=P)).then_inc(in_wo, 16)
            sp.dma_start(Mz[:, 0:DH], M).then_inc(in_mz, 16)
            sp.dma_start(Mz[:, DH:DH + 1], z.rearrange("(p a) -> p a", a=1)).then_inc(in_mz, 16)
            sp.dma_start(gtmp[:, 0:1], bass.AP(gate.tensor, 0, [[0, P], [1, 1]])).then_inc(in_gate, 16)
            sp.dma_start(srow_g[:], gu_scales.rearrange("g (t p) -> (g t) p", p=P)).then_inc(in_sc, 16)
            sp.dma_start(srow_d[:], dn_scales.rearrange("g (t p) -> (g t) p", p=P)).then_inc(in_sc, 16)
            sp.dma_start(kin[:], ssm).then_inc(in_k, 16)
            sp.dma_start(kd[:], ssm_d.rearrange("(p a) -> p a", a=1)).then_inc(in_k, 16)
            sp.dma_start(pk_g[:].rearrange("p (t c) -> p t c", t=OG),
                         gu_packed.rearrange("(t p) c -> p t c", p=P)).then_inc(in_pg, 16)
            sp.dma_start(pk_d[:].rearrange("p (t c) -> p t c", t=4),
                         dn_packed.rearrange("(t p) c -> p t c", p=P)).then_inc(in_pd, 16)
            sp.dma_start(xres[:], x[0].rearrange("(t p) d -> p t d", p=P)).then_inc(in_res, 16)
            sp.wait_ge(kernel_split, 4)
            sp.dma_start(toeplitz_rows, kpad[:]).then_inc(rows_stored, 16)
            sp.wait_ge(x_transposed, 2)
            sp.dma_start(xin[:], x[1].rearrange("(t p) d -> p t d", p=P)).then_inc(in_x, 16)
            with sp.Fori(1, B - 1) as i:
                xv = x.rearrange("b (t p) d -> b p t d", p=P)
                sp.wait_ge(x_transposed, i * 2 + 2)
                sp.dma_start(xin[:], xv[bass.ds(i + 1, 1)]).then_inc(in_x, 16)
                sp.wait_ge(z_made, i * 2)
                sp.dma_start(xres[:], xv[bass.ds(i, 1)]).then_inc(in_res, 16)
            sp.wait_ge(z_made, 2 * (B - 1))
            sp.dma_start(xres[:], x[B - 1].rearrange("(t p) d -> p t d", p=P)).then_inc(in_res, 16)
            sp.wait_ge(rows_stored, 16)

        @block.gpsimd
        def _(pool):
            nc.gpsimd.memset(ident[:], 0.0).then_inc(masks_made, 1)
            nc.gpsimd.memset(mask[:], 1.0).then_inc(masks_made, 1)
            nc.gpsimd.memset(halfneg[:], -0.5).then_inc(masks_made, 1)
            pool.wait_ge(masks_made, 3)
            nc.gpsimd.affine_select(out=ident[:], in_=ident[:], compare_op=ALU.not_equal, fill=1.0, base=0,
                                    pattern=[[-1, P]], channel_multiplier=1).then_inc(masks_made, 1)
            for k in (0, 2):
                m = mask[:, k * P:(k + 1) * P]
                nc.gpsimd.affine_select(out=m, in_=m, compare_op=ALU.is_ge, fill=0.0, base=0,
                                        pattern=[[1, P]], channel_multiplier=-1).then_inc(masks_made, 1)

            def slot(i):
                for n, k, kind, idx in weight_tiles(i):
                    if isinstance(i, int) and i == 1 and k == 0:
                        pool.wait_ge(unpacked, 20)
                        pool.wait_ge(wts_kept, 6)
                    wait(pool, w_transposed, n - 1)
                    src = v_g if kind == "g" else v_d
                    scale = sc_g[:, :, bass.ds(idx, 1)] if kind == "g" else \
                        sc_d[:, bass.ds(idx, 1), :].rearrange("p a t -> p t a")
                    for h in range(2):
                        done = nc.gpsimd.tensor_tensor(
                            w32[:, k % 2, :].rearrange("p (g c h j) -> p h g c j", g=4, h=2, j=4)[:, h],
                            src[:, bass.ds(idx * 512, 512)].rearrange("p (g c j h) -> p h g c j", g=4, h=2, j=4)[:, h],
                            scale.rearrange("p g (a b) -> p g a b", b=1).to_broadcast([P, 4, WD, 4]), ALU.mult)
                    done.then_inc(w_scaled, 1)
                if has(i, 1, B):
                    pool.wait_ge(stats, (i - 1) * 5 + 5)
                    nc.gpsimd.tensor_tensor(rs[:], ve[:], halfneg[:, 0:TT], ALU.pow).then_inc(rs_made, 1)

            rounds(pool, slot, 0, B + 1, *LOOP)

        @block.scalar
        def _(act):
            act.wait_ge(in_gate, 16)
            nc.scalar.activation(gtmp[:, 1:2], gtmp[:, 0:1], ACT.Exp, scale=-1.0).then_inc(gate_exp, 1)
            for m in range(3):
                act.wait_ge(wts_transposed, m + 1)
                nc.scalar.copy(wT[:, m, :, :], tr[m % 2][:].rearrange("p (k d) -> p k d", k=KD)).then_inc(wts_kept, 1)
            act.wait_ge(wts_transposed, 4)
            nc.scalar.copy(woT[:], tr[1][:]).then_inc(wts_kept, 1)
            act.wait_ge(wts_transposed, 5)
            nc.scalar.copy(sc_g[:].rearrange("p g t -> p (g t)"), tr[0][:, 0:KD * OG]).then_inc(wts_kept, 1)
            act.wait_ge(wts_transposed, 6)
            nc.scalar.copy(sc_d[:].rearrange("p g t -> p (g t)"), tr[1][:, 0:GI * 4]).then_inc(wts_kept, 1)

            def keep_xT(b):
                wait(act, x_transposed, at(b, 2, 1))
                wait(act, v_done, b)
                nc.scalar.copy(xT[:, 0:2, :].rearrange("p k t -> p (k t)"), tr[0][:]).then_inc(xT_a, 1)

            keep_xT(0)

            def slot(i):
                if has(i, 0, B - 1):
                    act.wait_ge(neg_made, i + 1)
                    nc.scalar.activation(neg[:], neg[:], ACT.Exp).then_inc(exp_made, 1)
                    act.wait_ge(v_done, i + 1)
                    wait(act, sums_done, i)
                    if isinstance(i, int) and i == 0:
                        act.wait_ge(consts, 2)
                    nc.scalar.copy(vext[:, :, 0:DH],
                                   p_v[:, 0:S].rearrange("p (t d) -> p t d", t=TT)).then_inc(v_kept, 1)
                if has(i, 1, B):
                    act.wait_ge(o_transposed, i)
                    wait(act, proj_done, i * 2 - 2)
                    nc.scalar.copy(oT[:], p_v[:, S:2 * S]).then_inc(oT_kept, 1)
                if has(i, 2, B + 1):
                    for t in range(TT):
                        act.wait_ge(x1_transposed, i * 2 - 4 + t + 1)
                        dst = x1T[:].rearrange("p (h m b j) -> p b m h j", m=4, b=8, j=8)[
                            :, bass.ds(i - 2, 1), :, t * 16:t * 16 + 16, :]
                        nc.scalar.copy(dst, tr[t][:].rearrange("p (a m h j) -> p a m h j", a=1, m=4, h=16)).then_inc(
                            x1T_kept, 1)
                if has(i, 0, B - 2):
                    keep_xT(i + 1)
                for n, k, kind, idx in weight_tiles(i):
                    act.wait_ge(w_transposed, n + 1)
                    if kind == "g":
                        dst = keep["wg_hi"][:, :, bass.ds(idx * P, P)]
                    else:
                        dst = keep["wd_hi"][:, bass.ds(idx, 1), :].rearrange("p a (t c) -> p (a t) c", t=4)
                    nc.scalar.copy(dst, tr[k % 2][:].rearrange("p (t c) -> p t c", t=4)).then_inc(w_high, 1)

            rounds(act, slot, 0, B + 1, *LOOP)

        @block.vector
        def _(dve):
            nc.vector.memset(kpad[:], 0.0).then_inc(kernel_split, 1)
            nc.vector.memset(vext[:], 1.0).then_inc(consts, 2)
            dve.wait_ge(in_sc, 32)
            nc.vector.tensor_scalar(srow_gf[:], srow_g[:], FP4_SHIFT, None, ALU.mult).then_inc(consts, 1)
            nc.vector.tensor_scalar(srow_df[:], srow_d[:], FP4_SHIFT, None, ALU.mult).then_inc(consts, 1)
            dve.wait_ge(in_k, 32)
            nc.vector.tensor_tensor(kin[:, 0:1], kin[:, 0:1], kd[:], ALU.add).then_inc(kernel_split, 1)
            dve.wait_ge(kernel_split, 2)
            nc.vector.tensor_copy(kpad[:, 0, P - 1:P - 1 + 512], kin[:]).then_inc(kernel_split, 1)
            dve.wait_ge(kernel_split, 3)
            nc.vector.tensor_tensor(kpad[:, 1, P - 1:P - 1 + 512], kin[:], kpad[:, 0, P - 1:P - 1 + 512],
                                    ALU.subtract).then_inc(kernel_split, 1)
            dve.wait_ge(gate_exp, 1)
            nc.vector.tensor_scalar_add(gtmp[:, 2:3], gtmp[:, 1:2], 1.0).then_inc(consts, 1)
            dve.wait_ge(consts, 5)
            nc.vector.reciprocal(gtmp[:, 3:4], gtmp[:, 2:3]).then_inc(consts, 1)
            dve.wait_ge(consts, 6)
            gv = gates[:].rearrange("p (t a) -> p t a", t=2)
            nc.vector.tensor_scalar(gv[:, :, 0], gtmp[:, 3:4].to_broadcast([P, 2]), -1.0, 1.0, ALU.mult,
                                    ALU.add).then_inc(consts, 1)
            nc.vector.tensor_copy(gv[:, :, 1], gtmp[:, 3:4].to_broadcast([P, 2])).then_inc(consts, 1)

            def keep_xT(b):
                wait(dve, x_transposed, at(b, 2, 2))
                wait(dve, v_done, b)
                nc.vector.tensor_copy(xT[:, 2:4, :].rearrange("p k t -> p (k t)"), tr[1][:]).then_inc(xT_v, 1)

            keep_xT(0)

            def unpack(packed, values, n, base):
                vals = values[:].bitcast(U32).rearrange("p (c j) -> p c j", j=4)
                for j in range(4):
                    low = 9 - 4 * j
                    wait(dve, unpacked, base + 2 * j)
                    nc.vector.tensor_scalar(sgn[:, 0:n], packed[:, 0:n], 12 - 4 * j, 0x80008000,
                                            ALU.logical_shift_left, ALU.bitwise_and)
                    nc.vector.tensor_scalar(mag[:, 0:n], packed[:, 0:n], abs(low), 0x0E000E00,
                                            ALU.logical_shift_left if low >= 0 else ALU.logical_shift_right,
                                            ALU.bitwise_and).then_inc(unpacked, 1)
                    dve.wait_ge(unpacked, base + 2 * j + 1)
                    nc.vector.tensor_tensor(vals[:, :, j], sgn[:, 0:n], mag[:, 0:n],
                                            ALU.bitwise_or).then_inc(unpacked, 1)

            def residual(b, t):
                dve.wait_ge(proj_done, b * 2 + t + 1)
                if t == 0:
                    dve.wait_ge(in_res, (b + 1) * 16)
                nc.vector.tensor_tensor(zs[:, t, :], p_out[:], xres[:, t, :], ALU.add).then_inc(z_made, 1)

            def slot(i):
                if has(i, 0, B - 1):
                    dve.wait_ge(qk_done, i + 1)
                    nc.vector.tensor_scalar_min(neg[:], p_qk[:], 0.0).then_inc(neg_made, 1)
                    dve.wait_ge(exp_made, i + 1)
                    nc.vector.scalar_tensor_tensor(out=sqk[:], in0=p_qk[:], scalar=0.0, in1=neg[:], op0=ALU.max,
                                                   op1=ALU.add).then_inc(sqk_made, 1)
                if isinstance(i, int) and i == 0:
                    dve.wait_ge(in_pg, 16)
                    unpack(pk_g, v_g, OG * WG, 0)
                    dve.wait_ge(in_pd, 16)
                    dve.wait_ge(unpacked, 8)
                    nc.vector.tensor_scalar(pk_dg.rearrange("p (g t c) -> p g t c", g=GI, t=4),
                                            pk_d[:].rearrange("p (t g c) -> p g t c", t=4, g=GI), 0, 0xFFFFFFFF,
                                            ALU.logical_shift_left, ALU.bitwise_and).then_inc(unpacked, 4)
                    dve.wait_ge(unpacked, 12)
                    unpack(pk_dg, v_d, GI * 4 * WD, 12)
                if has(i, 1, B):
                    residual(i - 1, 0)
                if has(i, 0, B - 2):
                    keep_xT(i + 1)
                if has(i, 1, B):
                    residual(i - 1, 1)
                if has(i, 0, B - 1):
                    dve.wait_ge(scores_done, i + 1)
                    if isinstance(i, int) and i == 0:
                        dve.wait_ge(masks_made, 6)
                    nc.vector.tensor_tensor(AT[:], p_sc[:, 0:3 * P], mask[:], ALU.mult).then_inc(masked, 1)
                if has(i, 1, B):
                    b = i - 1
                    for t in range(TT):
                        dve.wait_ge(z_made, b * 2 + t + 1)
                        nc.vector.bn_stats(st[:, t, :], zs[:, t, :]).then_inc(stats, 1)
                    for t in range(TT):
                        dve.wait_ge(stats, b * 5 + t + 1)
                        dve.sem_inc(seen, 1)
                        nc.vector.bn_aggr(mv[:, t, :], st[:, t, :]).then_inc(stats, 1)
                    dve.wait_ge(stats, b * 5 + 4)
                    nc.vector.tensor_scalar_add(ve[:], mv[:, :, 1], LN_EPS).then_inc(stats, 1)
                for n, k, kind, idx in weight_tiles(i):
                    dve.wait_ge(w_high, n + 1)
                    if kind == "g":
                        hi, lo = (keep[a][:, :, bass.ds(idx * P, P)] for a in ("wg_hi", "wg_lo"))
                    else:
                        hi, lo = (keep[a][:, bass.ds(idx, 1), :].rearrange("p a (t c) -> p (a t) c", t=4)
                                  for a in ("wd_hi", "wd_lo"))
                    nc.vector.tensor_tensor(lo, tr[k % 2][:].rearrange("p (t c) -> p t c", t=4), hi,
                                            ALU.subtract).then_inc(w_low, 1)
                if has(i, 1, B):
                    b = i - 1
                    dve.wait_ge(rs_made, b + 1)
                    wait(dve, x1_transposed, b * 2)
                    for t in range(TT):
                        nc.vector.tensor_scalar(x1n[:, t, :], zs[:, t, :], mv[:, t, 0:1], rs[:, t:t + 1],
                                                ALU.subtract, ALU.mult).then_inc(x1_made, 1)
                if has(i, 0, B - 1):
                    dve.wait_ge(sums_done, i + 1)
                    if isinstance(i, int) and i == 0:
                        dve.wait_ge(consts, 8)
                    for t in range(TT):
                        nc.vector.tensor_scalar_add(den[:, 2 * t:2 * t + 2], p_nm[t][:, DH:2 * DH + 2:DH + 1],
                                                    DEN_EPS).then_inc(o_steps, 1)
                    dve.wait_ge(o_steps, i * 8 + 2)
                    nc.vector.reciprocal(rden[:], den[:]).then_inc(o_steps, 1)
                    dve.wait_ge(o_steps, i * 8 + 3)
                    nc.vector.tensor_tensor(coef[:], rden[:], gates[:], ALU.mult).then_inc(o_steps, 1)
                    dve.wait_ge(o_steps, i * 8 + 4)
                    wait(dve, o_transposed, i)
                    for t in range(TT):
                        nc.vector.tensor_scalar(loc[:, t, :], p_nm[t][:, 0:DH], coef[:, 2 * t:2 * t + 1], None,
                                                ALU.mult).then_inc(o_steps, 1)
                    for t in range(TT):
                        dve.wait_ge(o_steps, i * 8 + 5 + t)
                        nc.vector.scalar_tensor_tensor(out=o[:, t, :], in0=p_nm[t][:, DH + 1:2 * DH + 1],
                                                       scalar=coef[:, 2 * t + 1:2 * t + 2], in1=loc[:, t, :],
                                                       op0=ALU.mult, op1=ALU.add).then_inc(o_steps, 1)

            rounds(dve, slot, 0, B + 1, *LOOP)

        @block.tensor
        def _(pe):
            def flip(dst, src, last=True):
                n = src.shape[0]
                return nc.tensor.matmul(dst, src, ident[0:n, 0:n], start=True, stop=True, is_transpose=True)

            pe.wait_ge(masks_made, 4)
            pe.wait_ge(in_w, 48)
            for m in range(3):
                wait(pe, wts_kept, m - 1)
                for k in range(KD):
                    done = flip(tr[m % 2][:, k * P:(k + 1) * P], wnat[:, m, k * P:(k + 1) * P])
                done.then_inc(wts_transposed, 1)
            pe.wait_ge(in_wo, 16)
            pe.wait_ge(wts_kept, 2)
            for k in range(KD):
                done = flip(tr[1][:, k * P:(k + 1) * P], wonat[:, k, :])
            done.then_inc(wts_transposed, 1)
            pe.wait_ge(consts, 4)
            pe.wait_ge(wts_kept, 3)
            flip(tr[0][:, 0:KD * OG], srow_gf[:]).then_inc(wts_transposed, 1)
            pe.wait_ge(wts_kept, 4)
            flip(tr[1][:, 0:GI * 4], srow_df[:]).then_inc(wts_transposed, 1)

            def transpose_x(b, i):
                wait(pe, in_x, b * 16 + 16)
                for h in range(2):
                    if isinstance(i, int) and i < 0:
                        pe.wait_ge(wts_kept, 5 + h)
                    elif has(i, 2, B + 1):
                        pe.wait_ge(x1T_kept, i * 2 - 4 + h + 1)
                    for k in range(2):
                        for t in range(TT):
                            done = flip(tr[h][:, (k * TT + t) * P:(k * TT + t + 1) * P],
                                        xin[:, t, (2 * h + k) * P:(2 * h + k + 1) * P])
                    done.then_inc(x_transposed, 1)

            transpose_x(0, -1)

            def project(b, t):
                wait(pe, z_made, b * 2 + t)
                nc.tensor.matmul(p_out[:], oT[:, t * P:(t + 1) * P], woT[:], start=True,
                                 stop=True).then_inc(proj_done, 1)

            def slot(i):
                if has(i, 0, B - 1):
                    pe.wait_ge(xT_a, i + 1)
                    pe.wait_ge(xT_v, i + 1)
                    wait(pe, sqk_made, i)
                    for m in range(2):
                        for k in range(KD):
                            done = nc.tensor.matmul(p_qk[:, m * S:(m + 1) * S], wT[:, m, k, :], xT[:, k, :],
                                                    start=(k == 0), stop=(k == KD - 1))
                    done.then_inc(qk_done, 1)
                    wait(pe, v_kept, i)
                    wait(pe, oT_kept, i - 1)
                    for t in range(TT):
                        for k in range(KD):
                            done = nc.tensor.matmul(p_v[:, t * DH:(t + 1) * DH], xT[:, k, t * P:(t + 1) * P],
                                                    wT[:, 2, k, :], start=(k == 0), stop=(k == KD - 1))
                    done.then_inc(v_done, 1)
                if has(i, 1, B):
                    pe.wait_ge(o_steps, i * 8)
                    if has(i, 0, B - 1):
                        pe.wait_ge(v_kept, i + 1)
                    for t in range(TT):
                        done = flip(p_v[:, S + t * P:S + (t + 1) * P], o[:, t, :])
                    done.then_inc(o_transposed, 1)
                if has(i, 2, B + 1):
                    wait(pe, w_low, i * 4 - 6)
                    for t in range(TT):
                        pe.wait_ge(x1_made, i * 2 - 4 + t + 1)
                        for k in range(KD):
                            done = flip(tr[t][:, k * P:(k + 1) * P], x1n[:, t, k * P:(k + 1) * P])
                        done.then_inc(x1_transposed, 1)
                if has(i, 1, B):
                    pe.wait_ge(oT_kept, i)
                    project(i - 1, 0)
                if has(i, 0, B - 2):
                    transpose_x(i + 1, i)
                if has(i, 1, B):
                    project(i - 1, 1)
                if has(i, 0, B - 1):
                    pe.wait_ge(sqk_made, i + 1)
                    wait(pe, masked, i)
                    nc.tensor.matmul(p_sc[:, 0:2 * P], sqk[:, S:S + P], sqk[:, 0:S], start=True, stop=True)
                    nc.tensor.matmul(p_sc[:, 2 * P:3 * P], sqk[:, S + P:2 * S], sqk[:, P:S], start=True,
                                     stop=True).then_inc(scores_done, 1)
                    if isinstance(i, int) and i == 0:
                        pe.wait_ge(in_mz, 32)
                    wait(pe, o_steps, i * 8)
                    for t in range(TT):
                        nc.tensor.matmul(p_nm[t][:, DH + 1:2 * DH + 2], sqk[:, t * P:(t + 1) * P], Mz[:],
                                         start=True, stop=True)
                for n, k, kind, idx in weight_tiles(i):
                    pe.wait_ge(w_scaled, n + 1)
                    if k >= 2:
                        pe.wait_ge(w_low, n - 1)
                    elif not has(i, 0, B - 2):
                        pe.wait_ge(x1T_kept, i * 2 - 4 + k + 1)
                    else:
                        pe.wait_ge((xT_a, xT_v)[k], i + 2)
                    for g in range(4):
                        done = flip(tr[k % 2][:, g * P:(g + 1) * P], w32[:, k % 2, g * P:(g + 1) * P])
                    done.then_inc(w_transposed, 1)
                if has(i, 0, B - 1):
                    pe.wait_ge(masked, i + 1)
                    pe.wait_ge(v_kept, i + 1)
                    nc.tensor.matmul(p_nm[0][:, 0:DH + 1], AT[:, 0:P], vext[:, 0, :], start=True, stop=True)
                    nc.tensor.matmul(p_nm[1][:, 0:DH + 1], AT[:, P:2 * P], vext[:, 0, :], start=True, stop=False)
                    nc.tensor.matmul(p_nm[1][:, 0:DH + 1], AT[:, 2 * P:3 * P], vext[:, 1, :], start=False,
                                     stop=True).then_inc(sums_done, 1)

            rounds(pe, slot, 0, B + 1, *LOOP)


def convolution_and_ffn(nc, sb, keep, ctx_in, toeplitz_rows, out, stack):
    B, S, D = ctx_in.shape
    NG, HG = 8, 4
    LB = D // P
    KD = D // P
    GI = 11
    GT = 2
    NT = GT * P

    def sem(name):
        return stack.enter_context(nc.semaphore(name))

    def psum(name):
        return stack.enter_context(nc.psum_tensor(name, [P, 512], F32))

    ident, x1T, halfneg = keep["ident"], keep["x1T"], keep["halfneg"]
    wg_hi, wg_lo, wd_hi, wd_lo = (keep[a] for a in ("wg_hi", "wg_lo", "wd_hi", "wd_lo"))

    toe = [sb(f"toe{p}", [P, 4, D], F16) for p in range(2)]
    cnat = [sb(f"cnat{p}", [P, D], F32) for p in range(2)]
    crev = sb("crev", [P, D], F32)
    kT = [sb(f"kT{p}", [P, 2 * LB * 64], F32) for p in range(2)]
    qv = [sb(f"qv{p}", [P, 2 * LB * 64], F32) for p in range(2)]
    qp = [sb(f"qp{p}", [P, LB * P], F32) for p in range(2)]
    kv32 = sb("kv32", [P, 9, LB, 32], F32)
    kv_hi = [sb(f"kv_hi{i}", [P, 9, LB, 32], F16) for i in range(2)]
    kv_lo = [sb(f"kv_lo{i}", [P, 9, LB, 32], F16) for i in range(2)]
    terms = [sb(f"terms{i}", [P, LB, 512], F32) for i in range(2)]
    R = [sb(f"R{p}", [P, LB * P], F32) for p in range(2)]
    x2n = sb("x2n", [P, GT, D], F32)
    x2hold = sb("x2hold", [P, GT, D], F32)
    x2_hi = sb("x2_hi", [P, KD, NT], F16)
    x2_lo = sb("x2_lo", [P, KD, NT], F16)
    sg = sb("sg", [P, 2, NT], F32)
    h32 = sb("h32", [P, 2, NT], F32)
    h_hi = sb("h_hi", [P, GI, NT], F16)
    h_lo = sb("h_lo", [P, GI, NT], F16)
    sq = sb("sq", [P, D], F32)
    z3 = sb("z3", [P, GT, D], F32)
    fin = sb("fin", [P, GT, D], F32)
    st2, mv2, ve2, rs2 = (sb(n, [P, GT, w], F32) for n, w in (("st2", 6), ("mv2", 2), ("ve2", 1), ("rs2", 1)))
    ss, ms, rr = (sb(n, [P, GT, 1], F32) for n in ("ss", "ms", "rr"))
    st3, mv3, ve3, rs3 = (sb(n, [P, GT, w], F32) for n, w in (("st3", 6), ("mv3", 2), ("ve3", 1), ("rs3", 1)))

    p_cv = [psum("p_cv0"), psum("p_cv1")]
    p_gu = [psum("p_gu0"), psum("p_gu1")]
    p_y = [psum("p_y0"), psum("p_y1")]
    p_ct, p_rt = psum("p_ct"), psum("p_rt")

    in_ctx = [sem(f"in_ctx{p}") for p in range(2)]
    in_toe = [sem(f"in_toe{p}") for p in range(2)]
    stored = [sem(f"stored{t}") for t in range(2)]
    ctx_reversed, ctx_flipped, kT_kept, q_kept = sem("ctx_reversed"), sem("ctx_flipped"), sem("kT_kept"), sem("q_kept")
    kv_made, kv_high, kv_low = sem("kv_made"), sem("kv_high"), sem("kv_low")
    convolved, termed, tree = sem("convolved"), sem("termed"), sem("tree")
    seen = sem("seen2")
    r_flipped, stats2, rs2_made, x2_made = sem("r_flipped"), sem("stats2"), sem("rs2_made"), sem("x2_made")
    x2_flipped, x2_high, x2_low, x2_held = sem("x2_flipped"), sem("x2_high"), sem("x2_low"), sem("x2_held")
    gu_done, silu_done, h_made, h_high, h_low = (sem(n) for n in
                                                 ("gu_done", "silu_done", "h_made", "h_high", "h_low"))
    y_done, y_squared, y_used, y_steps, rr_made, rs3_made, fin_made = (sem(n) for n in (
        "y_done", "y_squared", "y_used", "y_steps", "rr_made", "rs3_made", "fin_made"))

    ORDER = ["gu0", "c0", "gu1", "c1", "c2", "gu2", "c3", "gu3", "c4", "c5", "gu4", "ct0", "c6", "gu5", "c7", "c8",
             "gu6", "c9", "rt0", "gu7", "c10", "c11", "gu8", "c12", "c13", "gu9", "c14", "gu10", "ct1", "c15",
             "y0a", "rt1", "y0b", "xt0", "y1a", "xt1", "y1b"]

    def steps(conv, nxt, ffn):
        def on(s):
            if s[0] == "c" and s[1] != "t" or s[:2] in ("rt", "xt"):
                return conv
            return nxt if s[:2] == "ct" else ffn
        return [s for s in ORDER if on(s)]

    def iterations(engine, body):
        body(0, True, True, False)
        with engine.Fori(1, NG - 1) as it:
            body(it, True, True, True)
        body(NG - 1, True, False, True)
        body(NG, False, False, True)

    with nc.Block() as block:

        @block.sync
        def _(sp):
            rows = bass.AP(toeplitz_rows.tensor, 0, [[4 * 640, 16], [1, P], [640, 4], [1, D]])

            def load_ctx(g, p):
                sp.dma_start(cnat[p][:], ctx_in[:, bass.ds(g * 32 + p * 16, 16), :]).then_inc(in_ctx[p], 16)

            def load_toe(g, p):
                sp.dma_start(toe[p][:], rows[bass.ds(g * 2 + p, 1)]).then_inc(in_toe[p], 16)

            for p in range(2):
                load_ctx(0, p)
            for p in range(2):
                load_toe(0, p)
            for p in range(2):
                sp.wait_ge(ctx_reversed, p + 1)
                load_ctx(1, p)

            def body(it, conv, nxt, ffn):
                for p in range(2):
                    if nxt:
                        sp.wait_ge(convolved, it * 16 + 8 * p + 8)
                        load_toe(it + 1, p)
                    if nxt and not (isinstance(it, int) and it == NG - 2):
                        sp.wait_ge(ctx_reversed, it * 2 + 2 + p + 1)
                        load_ctx(it + 2, p)
                if ffn:
                    for t in range(GT):
                        sp.wait_ge(fin_made, (it - 1) * 2 + t + 1)
                        sp.dma_start(out[:, bass.ds((it - 1) * 32 + t * 16, 16), :], fin[:, t, :]).then_inc(
                            stored[t], 16)

            body(0, True, True, False)
            with sp.Fori(1, NG - 2) as it:
                body(it, True, True, True)
            body(NG - 2, True, True, True)
            body(NG - 1, True, False, True)
            body(NG, False, False, True)
            for t in range(GT):
                sp.wait_ge(stored[t], 16 * NG)

        @block.gpsimd
        def _(pool):
            def sum_terms(g, h):
                T = terms[h % 2]
                pool.wait_ge(termed, g * 16 + 4 * h + 4)
                nc.gpsimd.tensor_tensor(T[:, :, 0:256], T[:, :, 0:256], T[:, :, 256:512], ALU.add).then_inc(tree, 1)
                pool.wait_ge(tree, g * 12 + 3 * h + 1)
                nc.gpsimd.tensor_tensor(T[:, :, 0:128], T[:, :, 0:128], T[:, :, 128:256], ALU.add).then_inc(tree, 1)
                pool.wait_ge(tree, g * 12 + 3 * h + 2)
                wait(pool, r_flipped, g * 2 + h // 2 - 1)
                dst = R[h // 2][:].rearrange("p (m b e j) -> p m b e j", m=LB, b=B, e=2)[:, :, :, h % 2, :]
                a, b = (T[:, :, 64 * k:64 * k + 64].rearrange("p m (b j) -> p m b j", b=B) for k in range(2))
                nc.gpsimd.tensor_tensor(dst, a, b, ALU.add).then_inc(tree, 1)

            def root(src, dst, ready, count, made):
                pool.wait_ge(ready, count)
                nc.gpsimd.tensor_tensor(dst, src, halfneg[:, 0:1], ALU.pow).then_inc(made, 1)

            def low_part(f, i):
                pool.wait_ge(h_high, f * GI + i + 1)
                nc.gpsimd.tensor_tensor(h_lo[:, i, :], h32[:, i % 2, :], h_hi[:, i, :], ALU.subtract).then_inc(h_low, 1)

            def body(it, conv, nxt, ffn):
                g, f = it, it - 1
                for s in steps(conv, nxt, ffn):
                    if s[:2] == "gu" and int(s[2:]) >= 2:
                        low_part(f, int(s[2:]) - 2)
                    elif s in ("c3", "c7", "c11", "c15"):
                        sum_terms(g, int(s[1:]) // 4)
                    elif s[:2] == "rt":
                        t = int(s[2])
                        root(ve2[:, t], rs2[:, t], stats2, g * 6 + 3 * t + 3, rs2_made)
                    elif s == "y0a":
                        low_part(f, GI - 2)
                        low_part(f, GI - 1)
                    elif s in ("y1a", "y1b"):
                        t = int(s == "y1b")
                        root(ms[:, t], rr[:, t], y_steps, f * 8 + 4 * t + 1, rr_made)
                        root(ve3[:, t], rs3[:, t], y_steps, f * 8 + 4 * t + 4, rs3_made)

            iterations(pool, body)

        @block.scalar
        def _(act):
            def keep_kT(g, p):
                act.wait_ge(ctx_flipped, g * 2 + p + 1)
                wait(act, kv_made, (g - 1) * HG + 2 * p + 2)
                nc.scalar.copy(kT[p][:].rearrange("p (e r j) -> p e r j", e=2, j=8),
                               p_ct[:].rearrange("p (r e j) -> p e r j", e=2, j=8)).then_inc(kT_kept, 1)

            def reverse_ctx(g, p):
                act.wait_ge(in_ctx[p], (g + 1) * 16)
                wait(act, ctx_flipped, g * 2 + p)
                src = cnat[p][:]
                nc.scalar.copy(crev[:], bass.AP(src.tensor, src.offset + D - 1, [list(src.ap[0]), [-1, D]])).then_inc(
                    ctx_reversed, 1)

            def keep_q(g, p):
                wait(act, termed, (g - 1) * 16 + 8 * p + 8)
                wait(act, r_flipped, (g - 1) * 2 + p + 1)
                src = x1T[:, bass.ds(g * (HG * 256) + p * 512, 512)]
                nc.scalar.copy(qv[p][:], src)
                nc.scalar.copy(qp[p][:].rearrange("p (r e j) -> p e r j", e=2, j=8),
                               src.rearrange("p (e r j) -> p e r j", e=2, j=8)).then_inc(q_kept, 1)

            def high_kv(g, h):
                act.wait_ge(kv_made, g * HG + h + 1)
                wait(act, convolved, g * 16 + 4 * h - 4)
                nc.scalar.copy(kv_hi[h % 2][:], kv32[:]).then_inc(kv_high, 1)

            def high_h(f, i):
                act.wait_ge(h_made, f * GI + i + 1)
                nc.scalar.copy(h_hi[:, i, :], h32[:, i % 2, :]).then_inc(h_high, 1)

            for p in range(2):
                reverse_ctx(0, p)
                keep_kT(0, p)
                keep_q(0, p)
            high_kv(0, 0)

            def body(it, conv, nxt, ffn):
                g, f = it, it - 1
                if ffn:
                    act.wait_ge(x2_made, f * 2 + 2)
                    wait(act, y_used, f * 2)
                    nc.scalar.copy(x2hold[:], x2n[:]).then_inc(x2_held, 1)
                for s in steps(conv, nxt, ffn):
                    if s[:2] == "gu":
                        i = int(s[2:])
                        act.wait_ge(gu_done, f * GI + i + 1)
                        wait(act, h_made, f * GI + max(i - 1, 0))
                        nc.scalar.activation(sg[:, i % 2, :], p_gu[i % 2][:, 0:NT], ACT.Silu).then_inc(silu_done, 1)
                        if i == 0:
                            wait(act, y_done, f * 2)
                        else:
                            high_h(f, i - 1)
                        if i == GI - 1:
                            high_h(f, i)
                    elif s[:2] == "ct":
                        keep_kT(g + 1, int(s[2]))
                    elif s == "c1" and nxt or s == "c12" and nxt:
                        reverse_ctx(g + 1, int(s == "c12"))
                        if s == "c12":
                            high_kv(g + 1, 0)
                    elif s in ("c0", "c4", "c8"):
                        high_kv(g, int(s[1:]) // 4 + 1)
                    elif s[:2] == "rt" and nxt:
                        keep_q(g + 1, int(s[2]))
                    elif s[:2] == "xt":
                        t = int(s[2])
                        act.wait_ge(x2_flipped, g * 2 + t + 1)
                        nc.scalar.copy(x2_hi[:, :, t * P:(t + 1) * P],
                                       p_ct[:].rearrange("p (k c) -> p k c", k=KD)).then_inc(x2_high, 1)
                    elif s in ("y0b", "y1b"):
                        t = int(s == "y1b")
                        act.wait_ge(y_done, f * 2 + t + 1)
                        nc.scalar.activation(sq[:], p_y[t][:], ACT.Square,
                                             accum_out=ss[:, t]).then_inc(y_squared, 1)
                        act.wait_ge(y_squared, f * 2 + t + 1)

            iterations(act, body)

        @block.vector
        def _(dve):
            def products(g, h):
                K = kT[h // 2][:, 256 * (h % 2):256 * (h % 2) + 256]
                dve.wait_ge(kT_kept, g * 2 + h // 2 + 1)
                wait(dve, kv_low, g * HG + h)
                flat = kv32[:].rearrange("p r m c -> p r (m c)")
                kb = K.rearrange("p (r j) -> p r j", j=8)
                nc.vector.tensor_tensor(flat[:, 0:4].rearrange("p i (r j) -> p i r j", j=4),
                                        kb[:, :, 0:4].rearrange("p r (i a) -> p i r a", a=1).to_broadcast([P, 4, 32, 4]),
                                        kb[:, :, 4:8].rearrange("p (a r) j -> p a r j", a=1).to_broadcast([P, 4, 32, 4]),
                                        ALU.mult)
                k4 = K.rearrange("p (r j) -> p r j", j=4)
                nc.vector.tensor_tensor(flat[:, 4:6].rearrange("p i (r j) -> p i r j", j=2),
                                        k4[:, :, 0:2].rearrange("p r (i a) -> p i r a", a=1).to_broadcast([P, 2, 64, 2]),
                                        k4[:, :, 2:4].rearrange("p (a r) j -> p a r j", a=1).to_broadcast([P, 2, 64, 2]),
                                        ALU.mult)
                k2 = K.rearrange("p (r j) -> p j r", j=2)
                nc.vector.tensor_tensor(flat[:, 6:8], k2[:, 0:1].to_broadcast([P, 2, 128]), k2, ALU.mult)
                nc.vector.tensor_tensor(flat[:, 8], k2[:, 1], k2[:, 1], ALU.mult).then_inc(kv_made, 1)

            def low_kv(g, h):
                dve.wait_ge(kv_high, g * HG + h + 1)
                wait(dve, convolved, g * 16 + 4 * h - 4)
                nc.vector.tensor_tensor(kv_lo[h % 2][:], kv32[:], kv_hi[h % 2][:], ALU.subtract).then_inc(kv_low, 1)

            def make_terms(g, u):
                h, lb = u // 4, u % 4
                Y = p_cv[u % 2][:, 0:288].rearrange("p (r c) -> p r c", c=32)
                q = qv[h // 2][:, 256 * (h % 2) + 64 * lb:256 * (h % 2) + 64 * lb + 64]
                T = terms[h % 2][:, lb, :].rearrange("p (t c) -> p t c", t=8)
                dve.wait_ge(convolved, g * 16 + u + 1)
                if lb == 0:
                    dve.wait_ge(q_kept, g * 2 + h // 2 + 1)
                    wait(dve, tree, g * 12 + 3 * h - 3)
                q8 = q.rearrange("p (b j) -> p b j", j=8)
                T8 = T.rearrange("p t (b j) -> p t b j", j=8)
                Y4 = Y[:, 0:4].rearrange("p i (b j) -> p i b j", j=4)
                nc.vector.tensor_tensor(T8[:, 0:4, :, 4:8], Y4,
                                        q8[:, :, 0:4].rearrange("p b (i a) -> p i b a", a=1).to_broadcast([P, 4, 8, 4]),
                                        ALU.mult)
                nc.vector.tensor_tensor(T8[:, 0:4, :, 0:4].rearrange("p j b i -> p i b j"), Y4,
                                        q8[:, :, 4:8].rearrange("p (a b) j -> p a b j", a=1).to_broadcast([P, 4, 8, 4]),
                                        ALU.mult)
                q4 = q.rearrange("p (r j) -> p r j", j=4)
                T4 = T.rearrange("p t (r j) -> p t r j", j=4)
                Y2 = Y[:, 4:6].rearrange("p i (r j) -> p i r j", j=2)
                nc.vector.tensor_tensor(T4[:, 4:6, :, 2:4], Y2,
                                        q4[:, :, 0:2].rearrange("p r (i a) -> p i r a", a=1).to_broadcast([P, 2, 16, 2]),
                                        ALU.mult)
                nc.vector.tensor_tensor(T4[:, 4:6, :, 0:2].rearrange("p j r i -> p i r j"), Y2,
                                        q4[:, :, 2:4].rearrange("p (a r) j -> p a r j", a=1).to_broadcast([P, 2, 16, 2]),
                                        ALU.mult)
                base = p_cv[u % 2][:, 192:288]
                Y1 = bass.AP(base.tensor, base.offset, [list(base.ap[0]), [32, 2], [32, 2], [1, 32]])
                nc.vector.tensor_tensor(T[:, 6:8].rearrange("p t (r j) -> p t j r", j=2), Y1,
                                        q.rearrange("p (a r i) -> p i a r", a=1, i=2).to_broadcast([P, 2, 2, 32]),
                                        ALU.mult).then_inc(termed, 1)

            def norm_x2(g, t):
                dve.wait_ge(rs2_made, g * 2 + t + 1)
                if t == 0:
                    wait(dve, x2_held, g)
                nc.vector.tensor_scalar(x2n[:, t, :], p_rt[:], mv2[:, t, 0:1], rs2[:, t], ALU.subtract,
                                        ALU.mult).then_inc(x2_made, 1)

            def hidden(f, i):
                dve.wait_ge(silu_done, f * GI + i + 1)
                n = f * GI + max(i - 1, 0)
                wait(dve, h_high, n)
                wait(dve, h_low, n)
                nc.vector.scalar_tensor_tensor(out=h32[:, i % 2, :], in0=p_gu[i % 2][:, NT:2 * NT], scalar=H_SHIFT,
                                               in1=sg[:, i % 2, :], op0=ALU.mult, op1=ALU.mult).then_inc(h_made, 1)

            def finish(f, t):
                n = f * 8 + 4 * t
                dve.wait_ge(y_squared, f * 2 + t + 1)
                nc.vector.tensor_scalar(ms[:, t], ss[:, t], 1.0 / D, RMS_EPS * H_SHIFT * H_SHIFT, ALU.mult,
                                        ALU.add).then_inc(y_steps, 1)
                dve.wait_ge(rr_made, f * 2 + t + 1)
                dve.wait_ge(x2_held, f + 1)
                nc.vector.scalar_tensor_tensor(out=z3[:, t, :], in0=p_y[t][:], scalar=rr[:, t], in1=x2hold[:, t, :],
                                               op0=ALU.mult, op1=ALU.add).then_inc(y_used, 1)
                dve.wait_ge(y_used, f * 2 + t + 1)
                nc.vector.bn_stats(st3[:, t], z3[:, t, :]).then_inc(y_steps, 1)
                dve.wait_ge(y_steps, n + 2)
                dve.sem_inc(seen, 1)
                nc.vector.bn_aggr(mv3[:, t], st3[:, t]).then_inc(y_steps, 1)
                dve.wait_ge(y_steps, n + 3)
                nc.vector.tensor_scalar_add(ve3[:, t], mv3[:, t, 1:2], LN_EPS).then_inc(y_steps, 1)
                dve.wait_ge(rs3_made, f * 2 + t + 1)
                wait(dve, stored[t], f * 16)
                nc.vector.tensor_scalar(fin[:, t, :], z3[:, t, :], mv3[:, t, 0:1], rs3[:, t], ALU.subtract,
                                        ALU.mult).then_inc(fin_made, 1)

            products(0, 0)
            low_kv(0, 0)

            def body(it, conv, nxt, ffn):
                g, f = it, it - 1
                for s in steps(conv, nxt, ffn):
                    if s[:2] == "gu":
                        hidden(f, int(s[2:]))
                    elif s[0] == "c" and s[1] != "t":
                        u = int(s[1:])
                        h, lb = u // 4, u % 4
                        make_terms(g, u)
                        last = h == HG - 1
                        if lb == 0 and not last:
                            products(g, h + 1)
                        elif lb == 2 and not last:
                            low_kv(g, h + 1)
                        elif lb == 0 and nxt:
                            products(g + 1, 0)
                        elif lb == 2 and nxt:
                            low_kv(g + 1, 0)
                    elif s[:2] == "rt":
                        t = int(s[2])
                        n = g * 6 + 3 * t
                        dve.wait_ge(r_flipped, g * 2 + t + 1)
                        nc.vector.bn_stats(st2[:, t], p_rt[:]).then_inc(stats2, 1)
                        dve.wait_ge(stats2, n + 1)
                        dve.sem_inc(seen, 1)
                        nc.vector.bn_aggr(mv2[:, t], st2[:, t]).then_inc(stats2, 1)
                        dve.wait_ge(stats2, n + 2)
                        nc.vector.tensor_scalar_add(ve2[:, t], mv2[:, t, 1:2], LN_EPS).then_inc(stats2, 1)
                        norm_x2(g, t)
                    elif s[:2] == "xt":
                        t = int(s[2])
                        dve.wait_ge(x2_high, g * 2 + t + 1)
                        c = slice(t * P, (t + 1) * P)
                        nc.vector.tensor_tensor(x2_lo[:, :, c], p_ct[:].rearrange("p (k c) -> p k c", k=KD),
                                                x2_hi[:, :, c], ALU.subtract).then_inc(x2_low, 1)
                    elif s in ("y1a", "y1b"):
                        finish(f, int(s == "y1b"))

            iterations(dve, body)

        @block.tensor
        def _(pe):
            def flip(dst, src, stop=True):
                return nc.tensor.matmul(dst, src, ident[:], start=True, stop=stop, is_transpose=True)

            def flip_ctx(g, p):
                pe.wait_ge(ctx_reversed, g * 2 + p + 1)
                if p == 0:
                    wait(pe, x2_low, g * 2 - 2)
                else:
                    pe.wait_ge(kT_kept, g * 2 + 1)
                for k in range(LB):
                    done = flip(p_ct[:, k * P:(k + 1) * P], crev[:, (LB - 1 - k) * P:(LB - k) * P])
                done.then_inc(ctx_flipped, 1)

            def convolve(g, u):
                h, lb = u // 4, u % 4
                T = toe[h // 2]
                if lb == 0:
                    pe.wait_ge(kv_low, g * HG + h + 1)
                    if h % 2 == 0:
                        pe.wait_ge(in_toe[h // 2], (g + 1) * 16)
                wait(pe, termed, g * 16 + u - 1)
                for mb in range(lb + 1):
                    c = slice(P * (lb - mb), P * (lb - mb) + P)
                    hi, lo = T[:, 2 * (h % 2), c], T[:, 2 * (h % 2) + 1, c]
                    kh, kl = kv_hi[h % 2][:, :, mb, :], kv_lo[h % 2][:, :, mb, :]
                    nc.tensor.matmul(p_cv[u % 2][:, 0:288], hi, kh, start=(mb == 0), stop=False)
                    nc.tensor.matmul(p_cv[u % 2][:, 0:288], hi, kl, start=False, stop=False)
                    done = nc.tensor.matmul(p_cv[u % 2][:, 0:288], lo, kh, start=False, stop=(mb == lb))
                done.then_inc(convolved, 1)

            def gate_up(f, i):
                if i == 0:
                    pe.wait_ge(x2_low, f * 2 + 2)
                wait(pe, h_made, f * GI + max(i - 1, 0))
                for part, base in ((0, i * P), (1, (GI + i) * P)):
                    dst = p_gu[i % 2][:, part * NT:(part + 1) * NT]
                    for k in range(KD):
                        whi, wlo = wg_hi[:, k, base:base + P], wg_lo[:, k, base:base + P]
                        nc.tensor.matmul(dst, whi, x2_hi[:, k, :], start=(k == 0), stop=False)
                        nc.tensor.matmul(dst, whi, x2_lo[:, k, :], start=False, stop=False)
                        done = nc.tensor.matmul(dst, wlo, x2_hi[:, k, :], start=False, stop=(k == KD - 1))
                done.then_inc(gu_done, 1)

            def down(f, t, lo_i, hi_i):
                if lo_i == 0:
                    wait(pe, y_used, f * 2)
                c = slice(t * P, (t + 1) * P)
                for i in range(lo_i, hi_i):
                    pe.wait_ge(h_low, f * GI + i + 1)
                    nc.tensor.matmul(p_y[t][:], h_hi[:, i, c], wd_hi[:, i, :], start=(i == 0), stop=False)
                    nc.tensor.matmul(p_y[t][:], h_hi[:, i, c], wd_lo[:, i, :], start=False, stop=False)
                    done = nc.tensor.matmul(p_y[t][:], h_lo[:, i, c], wd_hi[:, i, :], start=False,
                                            stop=(i == GI - 1))
                if hi_i == GI:
                    done.then_inc(y_done, 1)

            for p in range(2):
                flip_ctx(0, p)

            def body(it, conv, nxt, ffn):
                g, f = it, it - 1
                for s in steps(conv, nxt, ffn):
                    if s[:2] == "gu":
                        gate_up(f, int(s[2:]))
                    elif s[:2] == "ct":
                        flip_ctx(g + 1, int(s[2]))
                    elif s[0] == "c":
                        convolve(g, int(s[1:]))
                    elif s[:2] == "rt":
                        t = int(s[2])
                        pe.wait_ge(tree, g * 12 + 6 * t + 6)
                        wait(pe, x2_made, g * 2 + t)
                        pe.wait_ge(q_kept, g * 2 + t + 1)
                        for k in range(LB):
                            c = slice(k * P, (k + 1) * P)
                            nc.tensor.matmul(p_rt[:, c], R[t][:, c], ident[:], start=True, stop=False,
                                             is_transpose=True)
                            done = nc.tensor.matmul(p_rt[:, c], qp[t][:, c], ident[:], start=False, stop=True,
                                                    is_transpose=True)
                        done.then_inc(r_flipped, 1)
                    elif s[:2] == "xt":
                        t = int(s[2])
                        pe.wait_ge(x2_made, g * 2 + t + 1)
                        if t == 1:
                            pe.wait_ge(x2_low, g * 2 + 1)
                        else:
                            wait(pe, kT_kept, g * 2 + 4 if nxt else g * 2 + 2)
                        for k in range(KD):
                            done = flip(p_ct[:, k * P:(k + 1) * P], x2n[:, t, k * P:(k + 1) * P])
                        done.then_inc(x2_flipped, 1)
                    elif s in ("y0a", "y1a"):
                        down(f, int(s[1]), 0, 6)
                    else:
                        down(f, int(s[1]), 6, GI)

            iterations(pe, body)


def decoder_layer(nc, x, ctx_2048, w_q, w_k, w_v, w_o, gate, M, z, ssm_kernel, ssm_d, gu_packed, gu_scales,
                  dn_packed, dn_scales, out):
    NH = ssm_kernel.shape[0]
    toeplitz_rows = nc.dram_tensor("toeplitz_rows", [NH, 2, 640], F16, kind="Internal").ap()
    with ExitStack() as outer:
        def kept(name, shape, dt):
            return outer.enter_context(nc.sbuf_tensor(name, shape, dt))

        keep = {
            "ident": kept("ident", [P, P], F32),
            "halfneg": kept("halfneg", [P, 2], F32),
            "x1T": kept("x1T", [P, NH * 256], F32),
            "wg_hi": kept("wg_hi", [P, 4, 2816], F16),
            "wg_lo": kept("wg_lo", [P, 4, 2816], F16),
            "wd_hi": kept("wd_hi", [P, 11, 512], F16),
            "wd_lo": kept("wd_lo", [P, 11, 512], F16),
        }
        with ExitStack() as stack:
            def sb(name, shape, dt):
                return stack.enter_context(nc.sbuf_tensor(name, shape, dt))
            attention_and_weights(nc, sb, keep, x, w_q, w_k, w_v, w_o, gate, M, z, ssm_kernel, ssm_d, gu_packed,
                                  gu_scales, dn_packed, dn_scales, toeplitz_rows, stack)
        with ExitStack() as stack:
            def sb(name, shape, dt):
                return stack.enter_context(nc.sbuf_tensor(name, shape, dt))
            convolution_and_ffn(nc, sb, keep, ctx_2048, toeplitz_rows, out, stack)


_INS = ['x', 'ctx_2048', 'L0_attn_w_q', 'L0_attn_w_k', 'L0_attn_w_v', 'L0_attn_w_o', 'L0_attn_gate', 'L0_attn_M',
        'L0_attn_z', 'L0_xattn_ssm_kernel', 'L0_xattn_D', 'L0_ffn_gate_up_packed', 'L0_ffn_gate_up_scales',
        'L0_ffn_down_packed', 'L0_ffn_down_scales']


def kernel(**inputs):
    import numpy as _np
    import concourse.bacc as _bacc
    from concourse import mybir as _mybir
    from concourse.bass_utils import run_bass_kernel_spmd as _run

    nc = _bacc.Bacc("TRN2", target_bir_lowering=False, num_devices=1)
    arrays, args = {}, []
    for name in _INS:
        a = _np.ascontiguousarray(inputs[name])
        if a.dtype == _np.int32:
            a = a.view(_np.uint32)
        arrays[f"in_{name}"] = a
        args.append(nc.dram_tensor(f"in_{name}", a.shape, _mybir.dt.from_np(a.dtype), kind="ExternalInput").ap())
    args.append(nc.dram_tensor("out_x", (8, 256, 512), _mybir.dt.float32, kind="ExternalOutput").ap())
    decoder_layer(nc, *args)
    r = _run(nc, [arrays], core_ids=[0])
    return r.results[0]["out_x"]
```
